# Optimizing a Trainium2 kernel written in Bass

```python
import numpy as np
import jax
import jax.numpy as jnp

def _softmax(x, axis=-1):
    return jax.nn.softmax(x, axis=axis)

def _gelu(x):
    return jax.nn.gelu(x, approximate=True)

def _silu(x):
    return jax.nn.silu(x)

def _sigmoid(x):
    return jax.nn.sigmoid(x)

def _layernorm(x, axis=-1, eps=1e-05):
    m = jnp.mean(x, axis=axis, keepdims=True)
    v = jnp.var(x, axis=axis, keepdims=True)
    return (x - m) / jnp.sqrt(v + eps)

def _scatter_add(tgt, idx, src, axis=0):
    return tgt.at[idx].add(src)

def _segment_sum(src, seg, n):
    return jax.ops.segment_sum(src, seg, n)
kernel_name = 'mk_gnn_preln_d2_gnn_r32_a1e572'

def setup_inputs(seed: int=0):
    np.random.seed(seed)
    _w = jnp.asarray

    def _rec_inputs():
        import jax
        import jax.numpy as jnp
        _gk = jax.random.key(seed)
        x = -4.129e-05 + 1 * jax.random.normal(jax.random.fold_in(_gk, 1), (3125, 128), jnp.float32)
        src = jax.random.randint(jax.random.fold_in(_gk, 2), (50000,), 0, 3125, jnp.int32)
        dst = jnp.minimum((3125 * jax.random.uniform(jax.random.fold_in(_gk, 3), (50000,)) ** 2.0).astype(jnp.int32), 99999)
        _o = jnp.argsort(dst, stable=True)
        src = src[_o]
        dst = dst[_o]
        edge_attr_16 = 0.000130101 + 1.00012 * jax.random.normal(jax.random.fold_in(_gk, 13), (50000, 16), jnp.float32)
        return (x, src, dst, edge_attr_16)
    x, src, dst, edge_attr_16 = _rec_inputs()

    def _L0_gnn_setup():
        import jax, jax.numpy as jnp
        import numpy as np
        N_NODES = 50000
        N_EDGES = 15625
        EMB_DIM = 128
        OUT_DIM = 128
        key = jax.random.key(seed)
        ks = jax.random.split(key, 6)
        batch = jax.random.randint(ks[0], (N_NODES,), 0, N_NODES, dtype=jnp.int64)
        src = jax.random.randint(ks[1], (N_EDGES,), 0, N_NODES, dtype=jnp.int64)
        dst = jax.random.randint(ks[2], (N_EDGES,), 0, N_NODES, dtype=jnp.int64)
        emb_table = jax.random.normal(ks[3], (N_NODES, EMB_DIM), dtype=jnp.float32)
        W1 = jax.random.normal(ks[4], (EMB_DIM, OUT_DIM), dtype=jnp.float32) / np.sqrt(EMB_DIM)
        b1 = jnp.zeros((OUT_DIM,), dtype=jnp.float32)
        W2 = jax.random.normal(ks[5], (OUT_DIM, OUT_DIM), dtype=jnp.float32) / np.sqrt(OUT_DIM)
        b2 = jnp.zeros((OUT_DIM,), dtype=jnp.float32)
        return {'batch': batch, 'src': src, 'dst': dst, 'emb_table': emb_table, 'W1': W1, 'b1': b1, 'W2': W2, 'b2': b2}
    _L0_gnn_all = _L0_gnn_setup()
    _L0_gnn_in = {k: v for k, v in _L0_gnn_all.items() if k in ('W1', 'b1', 'W2', 'b2')}
    del _L0_gnn_all

    def _L1_gnn_setup():
        import jax, jax.numpy as jnp
        import numpy as np
        HEADS = 2
        NEG_SLOPE = 0.2
        EPS = 1e-16

        def _gat_layer(x, src, dst, edge_attr_full, W, att, b, ew, eb):
            N, D = x.shape
            H = HEADS
            edge_emb = edge_attr_full @ ew.T + eb
            xw = x @ W
            xj = xw[src].reshape(-1, H, D) + edge_emb.reshape(-1, H, D)
            xi = xw[dst].reshape(-1, H, D)
            att_i, att_j = (att[:, :D], att[:, D:])
            alpha = jnp.einsum('ehd,hd->eh', xi, att_i) + jnp.einsum('ehd,hd->eh', xj, att_j)
            alpha = jax.nn.leaky_relu(alpha, NEG_SLOPE)
            amax = jax.ops.segment_max(alpha, dst, num_segments=N)
            ea = jnp.exp(alpha - amax[dst])
            denom = jax.ops.segment_sum(ea, dst, num_segments=N)
            alpha = ea / (denom[dst] + EPS)
            msg = xj * alpha[..., None]
            aggr = jax.ops.segment_sum(msg, dst, num_segments=N)
            return aggr.mean(axis=1) + b
        N, E, D, F = (10000, 10000, 128, 16)
        key = jax.random.key(seed)
        ks = jax.random.split(key, 8)
        return {'x': jax.random.normal(ks[0], (N, D), dtype=jnp.float32), 'edge_index': jax.random.randint(ks[1], (2, E), 0, N, dtype=jnp.int64), 'edge_attr': jax.random.normal(ks[2], (E, F), dtype=jnp.float32), 'weights': jax.random.normal(ks[3], (5, D, HEADS * D), dtype=jnp.float32) * 0.08, 'atts': jax.random.normal(ks[4], (5, HEADS, 2 * D), dtype=jnp.float32) * 0.08, 'biases': jnp.zeros((5, D), dtype=jnp.float32), 'edge_ws': jax.random.normal(ks[5], (5, HEADS * D, F), dtype=jnp.float32) * 0.2, 'edge_bs': jnp.zeros((5, HEADS * D), dtype=jnp.float32)}
    _L1_gnn_all = _L1_gnn_setup()
    _L1_gnn_in = {k: v for k, v in _L1_gnn_all.items() if k in ('weights', 'atts', 'biases', 'edge_ws', 'edge_bs')}
    del _L1_gnn_all
    return {'x': x, 'src': src, 'dst': dst, 'edge_attr_16': edge_attr_16, 'L0_gnn_W1': _L0_gnn_in['W1'], 'L0_gnn_b1': _L0_gnn_in['b1'], 'L0_gnn_W2': _L0_gnn_in['W2'], 'L0_gnn_b2': _L0_gnn_in['b2'], 'L1_gnn_weights': _L1_gnn_in['weights'], 'L1_gnn_atts': _L1_gnn_in['atts'], 'L1_gnn_biases': _L1_gnn_in['biases'], 'L1_gnn_edge_ws': _L1_gnn_in['edge_ws'], 'L1_gnn_edge_bs': _L1_gnn_in['edge_bs']}

def reference(x, src, dst, edge_attr_16, L0_gnn_W1, L0_gnn_b1, L0_gnn_W2, L0_gnn_b2, L1_gnn_weights, L1_gnn_atts, L1_gnn_biases, L1_gnn_edge_ws, L1_gnn_edge_bs):
    import jax
    import jax.numpy as jnp

    def _L0_gnn_ref(batch, src, dst, emb_table, W1, b1, W2, b2):
        import jax, jax.numpy as jnp
        import numpy as np
        N_NODES = 50000
        N_EDGES = 15625
        EMB_DIM = 128
        OUT_DIM = 128
        n = emb_table.shape[0]
        ones_e = jnp.ones(src.shape[0], dtype=emb_table.dtype)
        deg_out = jax.ops.segment_sum(ones_e, src, num_segments=n)
        deg_in = jax.ops.segment_sum(ones_e, dst, num_segments=n)
        norm_src = jax.lax.rsqrt(jnp.maximum(deg_out, 1.0))
        norm_dst = jax.lax.rsqrt(jnp.maximum(deg_in, 1.0))
        x = emb_table[batch]
        for W, b in ((W1, b1), (W2, b2)):
            h = x * norm_src[:, None]
            agg = jax.ops.segment_sum(h[src], dst, num_segments=n)
            agg = agg * norm_dst[:, None]
            x = jax.nn.relu(agg @ W + b)
        return x

    def _L1_gnn_ref(x, edge_index, edge_attr, weights, atts, biases, edge_ws, edge_bs):
        import jax, jax.numpy as jnp
        import numpy as np
        HEADS = 2
        NEG_SLOPE = 0.2
        EPS = 1e-16

        def _gat_layer(x, src, dst, edge_attr_full, W, att, b, ew, eb):
            N, D = x.shape
            H = HEADS
            edge_emb = edge_attr_full @ ew.T + eb
            xw = x @ W
            xj = xw[src].reshape(-1, H, D) + edge_emb.reshape(-1, H, D)
            xi = xw[dst].reshape(-1, H, D)
            att_i, att_j = (att[:, :D], att[:, D:])
            alpha = jnp.einsum('ehd,hd->eh', xi, att_i) + jnp.einsum('ehd,hd->eh', xj, att_j)
            alpha = jax.nn.leaky_relu(alpha, NEG_SLOPE)
            amax = jax.ops.segment_max(alpha, dst, num_segments=N)
            ea = jnp.exp(alpha - amax[dst])
            denom = jax.ops.segment_sum(ea, dst, num_segments=N)
            alpha = ea / (denom[dst] + EPS)
            msg = xj * alpha[..., None]
            aggr = jax.ops.segment_sum(msg, dst, num_segments=N)
            return aggr.mean(axis=1) + b
        N = x.shape[0]
        E = edge_index.shape[1]
        F = edge_attr.shape[1]
        loop = jnp.arange(N, dtype=edge_index.dtype)
        src = jnp.concatenate([edge_index[0], loop])
        dst = jnp.concatenate([edge_index[1], loop])
        edge_attr_full = jnp.concatenate([edge_attr, jnp.zeros((N, F), dtype=edge_attr.dtype)], axis=0)
        h = x
        for l in range(5):
            h = _gat_layer(h, src, dst, edge_attr_full, weights[l], atts[l], biases[l], edge_ws[l], edge_bs[l])
            if l < 4:
                h = jax.nn.relu(h)
        return h
    edge_index = jnp.stack([src, dst])
    batch0 = jnp.zeros((3125,), jnp.int32)
    h = jnp.maximum(_layernorm(x, axis=-1), 0.0)
    x = x + _L0_gnn_ref(batch0, src, dst, h, L0_gnn_W1, L0_gnn_b1, L0_gnn_W2, L0_gnn_b2)
    h = jnp.maximum(_layernorm(x, axis=-1), 0.0)
    x = x + _L1_gnn_ref(h, edge_index, edge_attr_16, L1_gnn_weights, L1_gnn_atts, L1_gnn_biases, L1_gnn_edge_ws, L1_gnn_edge_bs)
    return x

_drawn_inputs = setup_inputs


def setup_inputs(seed=0):
    import zlib

    import numpy as np

    out = dict(_drawn_inputs(seed))
    spreads = {'L0_gnn_b1': (0.0, 0.1),
     'L0_gnn_b2': (0.0, 0.1),
     'L1_gnn_biases': (0.0, 0.1),
     'L1_gnn_edge_bs': (0.0, 0.1)}
    factors = {}
    for name, (base, spread) in spreads.items():
        noise = np.random.default_rng([zlib.crc32(name.encode()), seed]).standard_normal(out[name].shape)
        drawn = base * np.exp(spread * noise) if base else spread * noise
        out[name] = jnp.asarray(drawn.astype(out[name].dtype))
    for name, factor in factors.items():
        out[name] = (out[name] * factor).astype(out[name].dtype)
    return out
```

```python
from contextlib import ExitStack

import concourse.bass as bass
from concourse import mybir

ALU = mybir.AluOpType
ACT = mybir.ActivationFunctionType
F32 = mybir.dt.float32
BF16 = mybir.dt.bfloat16
I32 = mybir.dt.int32
AX = mybir.AxisListType.X

P = 128
N = 3125
D = 128
E = 50000
H = 2
LAYERS = 5
FA = 16
NT = -(-N // P)
NP = NT * P
K = 28
CHUNKS = -(-E // (P * K))
TILES = K * CHUNKS
HK = H * K
GRP = 4
NG = K // GRP
WIN = 24
ROW = D + H
REG = 5
EC = FA + 1 + H
BIG = 1e30
LAST_BASE = NP - WIN
SLOPE = 0.2
LN_EPS = 1e-5
SM_EPS = 1e-16
PG = 7
NPG = TILES // PG
PAD_DST = 8191
NS0 = 384


def program(nc, x, src_rows, src_key, dst_col, dst_next_col, dst_flat, dst_first, dst_before,
            attr, W1, b1, W2, b2,
            weights, weightsT, attT, edge_w, edge_woT, biases, edge_b, out):
    with ExitStack() as ctx:
        def sb(name, shape, dt=F32):
            return ctx.enter_context(nc.sbuf_tensor(name, shape, dt))

        def sem(name):
            return ctx.enter_context(nc.semaphore(name))

        table = nc.dram_tensor("table", (NP, ROW), F32, kind="Internal").ap()
        ee_dram = nc.dram_tensor("ee_dram", (P, LAYERS * H * TILES), F32, kind="Internal").ap().rearrange(
            "p (l h t) -> p l h t", l=LAYERS, h=H)
        x_mid = nc.dram_tensor("x_mid", (NP, D), F32, kind="Internal").ap()
        table_pj = table.rearrange("(j p) f -> p j f", p=P)
        x_mid_pj = x_mid.rearrange("(j p) f -> p j f", p=P)
        x_pj = x.rearrange("(j p) f -> p j f", p=P)

        acc = sb("acc", [P, REG, NP])
        ai_rows = sb("ai_rows", [P, H, NP])
        rows = sb("rows", [P, 2, K, ROW])
        edge = sb("edge", [P, TILES, FA])
        ee = sb("ee", [P, H, TILES])
        ee_st = sb("ee_st", [P, LAYERS, H, K])
        edge_st = sb("edge_st", [P, K, EC])
        onehot = sb("onehot", [P, TILES, WIN], BF16)
        ai_win = sb("ai_win", [P, K, H, WIN])
        pw = sb("pw", [P, 2, GRP, 3, WIN])
        start_add = sb("start_add", [HK, CHUNKS, P], BF16)
        end_add = sb("end_add", [HK, CHUNKS, P], BF16)
        srci = sb("srci", [P, (CHUNKS + 2) * K], I32)
        idx_st = sb("idx_st", [P, 2, K], I32)
        bases = sb("bases", [1, (CHUNKS + 2) * K], I32)
        base_st = sb("base_st", [1, 2, K], I32)
        row_start = sb("row_start", [1, TILES], BF16)
        row_end = sb("row_end", [1, TILES], BF16)
        last_col = sb("last_col", [P, TILES], BF16)
        p2 = sb("p2", [P, K, H])
        alpha = sb("alpha", [P, 2, H, K])
        act_base = sb("act_base", [1, K], I32)
        fwd = sb("fwd", [HK, P])
        bwd = sb("bwd", [HK, P])
        carry_col = sb("carry_col", [HK, 2])
        crow = sb("crow", [1, H, K + 1])
        brow = sb("brow", [1, H, K + 1])
        cin = sb("cin", [1, 2, HK])
        phi = sb("phi", [1, 2, H])
        identf = sb("identf", [P, P])
        identb = sb("identb", [P, P], BF16)
        ones = sb("ones", [P, P])
        Wl = sb("Wl", [P, H * D])
        El = sb("El", [FA, H * D])
        ebl = sb("ebl", [P, H * D])
        biasl = sb("biasl", [P, D])
        V4 = sb("V4", [P, LAYERS, 4])
        v17 = sb("v17", [P, LAYERS, H, FA + 1])
        vb = sb("vb", [P, H, P])
        node4 = sb("node4", [P, NT, 4])
        noedge = sb("noedge", [P, NT])
        norm_dst = sb("norm_dst", [P, NT])
        c1 = sb("c1", [P, NT, H])
        c2 = sb("c2", [P, NT, H])
        sc = sb("sc", [P, 4, NT, H])
        hT = sb("hT", [P, 4, P])
        y = sb("y", [P, 2, D])
        stat = sb("stat", [P, 6])
        mv = sb("mv", [P, 4])
        eps = sb("eps", [P, 1])
        v4n = sb("v4n", [P, 4])
        v4c = sb("v4c", [P, 4])

        xt = rows[:, 0, 0:NT, :]
        prod = ai_win[:, :, :, :].rearrange("p k h w -> p (k h w)")[:, 2 * D:2 * D + H * K * FA].rearrange(
            "p (h k f) -> p h k f", h=H, k=K)

        accf = acc[:, :, :].rearrange("p r n -> p (r n)")
        aif = ai_rows[:, :, :].rearrange("p r n -> p (r n)")
        rowsf = rows[:, :, :, :].rearrange("p a b c -> p (a b c)")
        cut = [0]

        def part(base, n, dt=F32):
            words = n if dt != BF16 else (n + 1) // 2
            v = base[:, cut[0]:cut[0] + words]
            cut[0] += words
            return v if dt == F32 else v.bitcast(dt)[:, 0:n]

        attr_in = part(accf, TILES * FA)[:, :].rearrange("p (t f) -> p t f", f=FA)
        key_i = part(accf, TILES, I32)
        lo_i = part(accf, TILES, I32)
        hi_i = part(accf, TILES, I32)
        dstc_i = part(accf, TILES, I32)
        dstn_i = part(accf, TILES, I32)
        dst_f = part(accf, TILES)
        dstn_f = part(accf, TILES)
        deg_e = part(accf, TILES)
        n_e = part(accf, TILES)
        r_e = part(accf, TILES)
        row0_i = part(accf, TILES + 1, I32)
        row1_i = part(accf, TILES + 1, I32)
        row0_f = part(accf, TILES + 1)
        row1_f = part(accf, TILES + 1)
        WT0 = cut[0]
        far0 = WT0 + LAYERS * H * P
        cut[0] = 0
        oh_lo = part(rowsf, 2 * PG * P, BF16).rearrange("p (b t l) -> p b t l", b=2, t=PG)
        oh_loT = part(rowsf, 2 * PG * P, BF16).rearrange("p (b t l) -> p b t l", b=2, t=PG)
        wparts = part(rowsf, 2 * PG * 4 * NT, BF16).rearrange("p (b t q h) -> p b t q h", b=2, t=PG, q=4)
        picked = part(rowsf, PG * NT).rearrange("p (t h) -> p t h", t=PG)
        parts4 = part(rowsf, TILES * 4, BF16).rearrange("p (t q) -> p t q", q=4)
        lo_s = part(rowsf, TILES + PG, BF16)
        hi_s = part(rowsf, TILES, BF16)
        lo_d = part(rowsf, TILES, BF16)
        hi_d = part(rowsf, TILES, BF16)
        degp = part(rowsf, 2 * NT, BF16).rearrange("p (q h) -> p q h", q=2)
        deg_i = part(rowsf, 3 * NT, I32).rearrange("p (q h) -> p q h", q=3)
        iota_i = part(rowsf, P, I32)
        iota_b = part(rowsf, P, BF16)
        zeros_b = part(rowsf, P, BF16)
        assert cut[0] <= 2 * K * ROW
        cut[0] = 0
        rcur = part(aif, CHUNKS * P, I32).rearrange("p (c e) -> p c e", e=P)
        rprev = part(aif, CHUNKS * P, I32).rearrange("p (c e) -> p c e", e=P)
        rnext = part(aif, CHUNKS * P, I32).rearrange("p (c e) -> p c e", e=P)
        cut[0] = 0
        oh_hi_s = part(aif, TILES * NT, BF16).rearrange("p (t h) -> p t h", h=NT)
        cut[0] = 0
        oh_hi_d = part(accf, TILES * NT, BF16).rearrange("p (t h) -> p t h", h=NT)
        assert cut[0] <= TILES * FA
        far = accf[:, far0:REG * NP]
        cut[0] = 0
        norm_src = part(far, NT)
        s_deg = part(far, 4 * NT)
        s_nd = part(far, NT)
        w1s = part(far, D)
        b1s = part(far, D)
        gs = part(far, D)
        h0 = part(far, D)
        h0T = part(far, 1)
        h0b = part(far, P)
        xrow = part(far, D)
        us = part(far, D)
        attb = part(far, P)
        ewo = part(far, LAYERS * H * (FA + 1)).rearrange("p (l h k) -> p l h k", l=LAYERS, h=H)
        attTs = part(far, LAYERS * 4).rearrange("p (l q) -> p l q", l=LAYERS)
        assert cut[0] <= REG * NP - far0
        WTs = accf[:, WT0:WT0 + LAYERS * H * P].rearrange("p (l h f) -> p l h f", l=LAYERS, h=H)
        w2s = ai_win[:, :, :, :].rearrange("p k h w -> p (k h w)")[:, 0:D]
        b2s = ai_win[:, :, :, :].rearrange("p k h w -> p (k h w)")[:, D:2 * D]

        bank = [ctx.enter_context(nc.psum_tensor(f"bank{i}", [P, 512], F32)) for i in range(8)]

        def grp_sum(g, k):
            return bank[g][:, k * REG * WIN:(k + 1) * REG * WIN]

        loaded = sem("loaded")
        loaded_rows = sem("loaded_rows")
        made = sem("made")
        lay_w = sem("lay_w")
        step = sem("step")
        added = sem("added")
        passed = {e: sem(f"passed_{e}") for e in ("dve", "act", "pe", "pool", "sp")}
        att_spread = sem("att_spread")
        oh_ready = sem("oh_ready")
        oh_used = sem("oh_used")
        ohT_ps = sem("ohT_ps")
        ohT_sb = sem("ohT_sb")
        look_ps = sem("look_ps")
        look_used = sem("look_used")
        dve_pre = sem("dve_pre")
        pe_pre = sem("pe_pre")
        act_pre = sem("act_pre")
        gath = [sem("gath0"), sem("gath1")]
        idx_ready = sem("idx_ready")
        rows_free = sem("rows_free")
        table_w = sem("table_w")
        xt_in = sem("xt_in")
        xmid_in = sem("xmid_in")
        x2_ready = sem("x2_ready")
        xmid_w = sem("xmid_w")
        ln_stat = sem("ln_stat")
        ln_std = sem("ln_std")
        ln_coef = sem("ln_coef")
        ee_ready = sem("ee_ready")
        ee_w = sem("ee_w")
        ee_free = sem("ee_free")
        ee_in = sem("ee_in")
        oh_f = sem("oh_f")
        est_ready = sem("est_ready")
        abase = sem("abase")
        acc_zero = sem("acc_zero")
        win_ready = sem("win_ready")
        win_used = sem("win_used")
        al_ready = sem("al_ready")
        al_ps = sem("al_ps")
        scan1 = sem("scan1")
        row_ps = sem("row_ps")
        scan2 = sem("scan2")
        col_ps = sem("col_ps")
        diff = sem("diff")
        expd = sem("expd")
        t_ps = sem("t_ps")
        p_sb = sem("p_sb")
        phi_ps = sem("phi_ps")
        p_ready = sem("p_ready")
        sums = sem("sums")
        sums_free = sem("sums_free")
        chunk_done = sem("chunk_done")
        nsc_ps = sem("nsc_ps")
        nsc_m = sem("nsc_m")
        nsc_e = sem("nsc_e")
        coef = sem("coef")
        old_ps = sem("old_ps")
        old_sb = sem("old_sb")
        y_ps = sem("y_ps")
        y_sb = sem("y_sb")
        h_sb = sem("h_sb")
        new_ps = sem("new_ps")
        new_sb = sem("new_sb")
        ai_ps = sem("ai_ps")
        ai_sb = sem("ai_sb")
        row_done = sem("row_done")
        vb_ready = sem("vb_ready")
        out_w = sem("out_w")

        block = ctx.enter_context(nc.Block())
        PRE_LOADS = [(srci[:, :], src_rows), (key_i, src_key), (dstc_i, dst_col), (dstn_i, dst_next_col),
                     (attr_in.rearrange("p t f -> p (t f)"), attr),
                     (row0_i[0:1, :], dst_first),
                     (row1_i[0:1, :], dst_before),
                     (w1s, W1), (b1s, b1.rearrange("(o d) -> o d", o=1).broadcast_to((P, D))),
                     (w2s, W2), (b2s, b2.rearrange("(o d) -> o d", o=1).broadcast_to((P, D))),
                     (xrow[0:1, :], x[0:1, :]),
                     (WTs.rearrange("p l h f -> p (l h f)"), weightsT),
                     (attTs.rearrange("p l q -> p (l q)"), attT),
                     (ewo.rearrange("p l h k -> p (l h k)"), edge_woT)]
        N_LOADS = 16 * len(PRE_LOADS)

        def rounds(eng, body):
            with eng.Fori(0, LAYERS - 1) as layer:
                body(layer, False)
            body(LAYERS - 1, True)

        def chunk_pairs(eng, first, body, peel=False):
            pairs = CHUNKS // 2
            with eng.Fori(0, pairs - 1 if peel else pairs) as i:
                for b in range(2):
                    body(i, b, first + 2 * i + b, 2 * i + b)
            if peel:
                for b in range(2):
                    body(pairs - 1, b, first + 2 * (pairs - 1) + b, CHUNKS - 2 + b)

        def q0(layer):
            return (layer + 1) * CHUNKS

        def n0(layer):
            return layer * NT

        @block.sync
        def _(sp):
            for dst, s in PRE_LOADS:
                sp.dma_start(dst, s).then_inc(loaded, 16)
            for hh in range(H):
                for dst, off in ((rcur, 1), (rprev, 0), (rnext, 2)):
                    v = dst_flat[0, off:off + TILES * P].rearrange("(c r e) -> r c e", r=K, e=P)
                    sp.dma_start(dst[hh * K:(hh + 1) * K], v).then_inc(loaded_rows, 16)
            for j in range(NT):
                sp.wait_ge(act_pre, 5 + j)
                sp.dma_start(table_pj[:, j, :], xt[:, j, :]).then_inc(table_w, 16)

            def layer_weights(layer):
                sp.dma_start(Wl[:, :], weights[bass.ds(layer * P, P), :]).then_inc(lay_w, 16)
                sp.dma_start(El[:, :], edge_w[bass.ds(layer * FA, FA), :]).then_inc(lay_w, 16)
                sp.dma_start(ebl[:, :], edge_b[bass.ds(layer, 1), :].broadcast_to((P, H * D))).then_inc(lay_w, 16)
                sp.dma_start(biasl[:, :], biases[bass.ds(layer, 1), :].broadcast_to((P, D))).then_inc(lay_w, 16)

            def table_tiles(n):
                for j in range(NT):
                    sp.wait_ge(row_done, n + j + 1)
                    sp.sem_inc(passed["sp"], 1)
                    sp.dma_start(table_pj[:, j, :], xt[:, j, :]).then_inc(table_w, 16)

            layer_weights(0)
            sp.sem_inc(ee_free, 1)

            def ee_out(i, b, q, c):
                sp.wait_ge(ee_ready, q + 1)
                sp.sem_inc(passed["sp"], 1)
                sp.dma_start(ee_dram[:, :, :, bass.ds(c * K, K)], ee_st[:, :, :, :]).then_inc(ee_w, 16)
                sp.wait_ge(ee_w, 16 * (q + 1))
                sp.sem_inc(ee_free, 1)

            chunk_pairs(sp, 0, ee_out)
            sp.dma_start(ee[:, :, :], ee_dram[:, 0, :, :]).then_inc(ee_in, 16)
            sp.wait_ge(rows_free, CHUNKS + 1)
            sp.dma_start(xt[:, :, 0:D], x_pj).then_inc(xt_in, 16)
            sp.wait_ge(x2_ready, 1)
            sp.dma_start(x_mid_pj, xt[:, :, 0:D]).then_inc(xmid_w, 16)
            table_tiles(0)

            def gat(layer, final):
                sp.wait_ge(rows_free, q0(layer) + CHUNKS + 1)
                sp.wait_ge(table_w, 16 * NT * (layer + 2))
                sp.sem_inc(passed["sp"], 1)
                sp.dma_start(xt[:, :, :], table_pj).then_inc(xt_in, 16)
                if final:
                    sp.wait_ge(rows_free, q0(layer) + CHUNKS + 2)
                    sp.wait_ge(xmid_w, 16)
                    sp.dma_start(rows[:, 1, 0:NT, 0:D], x_mid_pj).then_inc(xmid_in, 16)
                    for j in range(NT):
                        n = P if j < NT - 1 else N - (NT - 1) * P
                        sp.wait_ge(row_done, n0(layer + 1) + j + 1)
                        sp.dma_start(out[j * P:j * P + n, :], xt[0:n, j, 0:D]).then_inc(out_w, 16)
                else:
                    sp.wait_ge(chunk_done, q0(layer) + CHUNKS)
                    sp.sem_inc(passed["sp"], 1)
                    sp.dma_start(ee[:, :, :], ee_dram[:, bass.ds(layer + 1, 1), :, :].rearrange("p l h t -> p (l h) t"))\
                        .then_inc(ee_in, 16)
                    table_tiles(n0(layer + 1))
                    layer_weights(layer + 1)

            rounds(sp, gat)
            sp.wait_ge(out_w, 16 * NT)

        @block.gpsimd
        def _(pool):
            nc.gpsimd.memset(ones[:, :], 1.0).then_inc(made, 1)
            nc.gpsimd.memset(identf[:, :], 0.0).then_inc(made, 1)
            nc.gpsimd.iota(iota_i, [[1, P]], base=0, channel_multiplier=0).then_inc(made, 1)
            pool.wait_ge(made, 3)
            nc.gpsimd.affine_select(out=identf[:, :], in_=identf[:, :], compare_op=ALU.not_equal, fill=1.0,
                                    base=0, pattern=[[-1, P]], channel_multiplier=1).then_inc(made, 1)

            def gather(first, tables):
                def body(i, b, q, c):
                    pool.wait_ge(idx_ready, q + 1)
                    pool.wait_ge(rows_free, q + 1)
                    pool.wait_ge(table_w, tables)
                    pool.sem_inc(passed["pool"], 1)
                    for k in range(K):
                        nc.gpsimd.indirect_dma_start(
                            out=rows[:, b, k, :], out_offset=None, in_=table,
                            in_offset=bass.IndirectOffsetOnAxis(ap=idx_st[:, b, k:k + 1], axis=0),
                        ).then_inc(gath[b], 16)
                chunk_pairs(pool, first, body)

            def clear(done):
                for j in range(NT):
                    pool.wait_ge(y_ps, done + j + 1)
                    pool.sem_inc(passed["pool"], 1)
                    nc.gpsimd.memset(acc[:, :, j * P:(j + 1) * P], 0.0).then_inc(acc_zero, 1)

            gather(0, 16 * NT)
            clear(0)

            def gat(layer, final):
                gather(q0(layer), 16 * NT * (layer + 2))
                if not final:
                    clear(n0(layer + 1))

            rounds(pool, gat)

        @block.scalar
        def _(act):
            with act.Fori(0, NPG // 2) as i:
                for b in range(2):
                    g = 2 * i + b
                    act.wait_ge(ohT_ps, g + 1)
                    act.wait_ge(look_used, g + 1)
                    nc.scalar.copy(oh_loT[:, b, :, :].rearrange("p t l -> p (t l)"),
                                   bank[4 + b][:, 0:PG * P // 2].bitcast(BF16)).then_inc(ohT_sb, 1)
            act.wait_ge(dve_pre, 4)
            nc.scalar.activation(n_e, n_e, ACT.Sqrt).then_inc(act_pre, 1)
            act.wait_ge(dve_pre, 6)
            nc.scalar.activation(s_deg[:, 3 * NT:4 * NT], s_deg[:, 3 * NT:4 * NT], ACT.Sqrt).then_inc(act_pre, 1)
            nc.scalar.activation(norm_src, norm_src, ACT.Sqrt).then_inc(act_pre, 1)
            nc.scalar.activation(mv[0:1, 2:3], mv[0:1, 1:2], ACT.Sqrt, bias=eps[0:1, :]).then_inc(act_pre, 1)
            for j in range(NT):
                act.wait_ge(dve_pre, 11 + j)
                nc.scalar.activation(xt[:, j, 0:D], y[:, j % 2, :], ACT.Relu,
                                     scale=norm_src[:, j:j + 1]).then_inc(act_pre, 1)

            def copy_new(j, n):
                act.wait_ge(new_ps, n + j + 1)
                nc.scalar.copy(hT[:, 2 + j % 2, :], bank[7][:, 0:P]).then_inc(new_sb, 1)

            def copy_ai(j, n):
                act.wait_ge(ai_ps, n + j + 1)
                nc.scalar.copy(ai_rows[:, :, j * P:(j + 1) * P],
                               bank[2 + j % 2][:, 0:2 * P].rearrange("p (h n) -> p h n", h=H)).then_inc(ai_sb, 1)

            def gcn_chunk(i, b, q, c):
                for g in range(NG):
                    act.wait_ge(sums_free, q * NG + g + 1)
                    nc.scalar.copy(pw[:, (b + g) % 2, :, 0, :],
                                   onehot[:, bass.ds(c * K + g * GRP, GRP), :]).then_inc(oh_f, 1)

            chunk_pairs(act, 0, gcn_chunk)
            act.wait_ge(ln_stat, 1)
            nc.scalar.activation(sc[:, 1, :, 0], sc[:, 0, :, 1], ACT.Sqrt, bias=eps[:, :]).then_inc(ln_std, 1)
            act.wait_ge(ln_coef, 1)
            act.wait_ge(xmid_w, 16)
            for s in range(NT + 2):
                if s < NT:
                    nc.scalar.activation(xt[:, s, 0:D], xt[:, s, 0:D], ACT.Relu, scale=sc[:, 2, s, 0:1],
                                         bias=sc[:, 3, s, 0:1]).then_inc(h_sb, 1)
                if 0 <= s - 1 < NT:
                    copy_new(s - 1, 0)
                if 0 <= s - 2 < NT:
                    copy_ai(s - 2, 0)

            def gat(layer, final):
                act.wait_ge(ai_sb, (layer + 1) * NT)

                def stage(c, n):
                    act.wait_ge(win_used, n + 1)
                    act.sem_inc(passed["act"], 1)
                    nc.scalar.copy(act_base[:, :], bases[:, bass.ds(c * K, K)]).then_inc(abase, 1)
                    act.wait_ge(abase, n + 1)
                    act.sem_inc(passed["act"], 1)

                def windows(first, last):
                    for k in range(first, last):
                        base = nc.values_load(act_base[0:1, k:k + 1], engines=(mybir.EngineType.Activation,),
                                              min_val=0, max_val=LAST_BASE,
                                              skip_runtime_bounds_check_because="clamped on the chip")
                        ins = nc.scalar.copy(ai_win[:, k, :, :], ai_rows[:, :, bass.ds(base, WIN)])
                        if k == K - 1:
                            ins.then_inc(win_ready, 1)

                for c in range(2):
                    stage(c, layer * CHUNKS + c)
                    windows(0, K)

                def body(i, b, q, c):
                    cq = layer * CHUNKS + c
                    ahead = not isinstance(c, int)
                    act.wait_ge(sums_free, q * NG + 2)
                    act.sem_inc(passed["act"], 1)
                    nc.scalar.copy(edge_st[:, :, 0:FA], edge[:, bass.ds(c * K, K), :]).then_inc(est_ready, 1)
                    for g in range(2):
                        nc.scalar.copy(pw[:, (b + g) % 2, :, 2, :],
                                       onehot[:, bass.ds(c * K + g * GRP, GRP), :]).then_inc(oh_f, 1)
                    act.wait_ge(diff, 2 * cq + 1)
                    nc.scalar.activation(phi[:, 1, :], phi[:, 0, :], ACT.Exp).then_inc(expd, 1)
                    act.wait_ge(diff, 2 * cq + 2)
                    nc.scalar.activation(bwd[:, :], bwd[:, :], ACT.Exp).then_inc(expd, 1)
                    if ahead:
                        stage(c + 2, cq + 2)
                    for g in range(NG):
                        if ahead:
                            windows(g * GRP, (g + 1) * GRP)
                        if g >= 2:
                            act.wait_ge(sums_free, q * NG + g + 1)
                            nc.scalar.copy(pw[:, (b + g) % 2, :, 2, :],
                                           onehot[:, bass.ds(c * K + g * GRP, GRP), :]).then_inc(oh_f, 1)

                chunk_pairs(act, q0(layer), body, peel=True)
                act.wait_ge(nsc_m, layer + 1)
                nc.scalar.activation(sc[:, 2:4, :, :].rearrange("p a j h -> p (a j h)"),
                                     sc[:, 2:4, :, :].rearrange("p a j h -> p (a j h)"), ACT.Exp).then_inc(nsc_e, 1)
                n = n0(layer + 1)
                for s in range(-1, NT + (0 if final else 2)):
                    if not final:
                        if 0 <= s - 1 < NT:
                            act.wait_ge(y_sb, n + s)
                            nc.scalar.activation(xt[:, s - 1, 0:D], y[:, (s - 1) % 2, :], ACT.Relu).then_inc(h_sb, 1)
                        if 0 <= s - 2 < NT:
                            copy_ai(s - 2, n)
                        if 0 <= s - 1 < NT:
                            copy_new(s - 1, n)
                    if s + 1 < NT:
                        act.wait_ge(old_ps, n0(layer) + s + 2)
                        nc.scalar.copy(hT[:, (s + 1) % 2, :], bank[6][:, 0:P]).then_inc(old_sb, 1)

            rounds(act, gat)

        @block.tensor
        def _(pe):
            pe.wait_ge(made, 4)
            pe.wait_ge(loaded, N_LOADS)
            pe.wait_ge(dve_pre, 1)
            for l in range(LAYERS):
                for h in range(H):
                    nc.tensor.matmul(bank[0][:, (l * H + h) * 2:(l * H + h) * 2 + 2], WTs[:, l, h, :],
                                     attTs[:, l, 2 * h:2 * h + 2], start=True, stop=True)
            nc.tensor.matmul(bank[1][:, 0:TILES], ones[0:1, :], row0_f[0:1, 0:TILES], start=True, stop=True)\
                .then_inc(pe_pre, 1)
            for l in range(LAYERS):
                for h in range(H):
                    n = l * H + h
                    pe.wait_ge(att_spread, n + 1)
                    nc.tensor.matmul(bank[2][:, n * (FA + 1):(n + 1) * (FA + 1)], attb, ewo[:, l, h, :],
                                     start=True, stop=True).then_inc(pe_pre, 1)
            pe.wait_ge(dve_pre, 2)
            nc.tensor.matmul(bank[3][:, 0:NT], zeros_b, zeros_b[:, 0:NT],
                             start=True, stop=False, skip_group_check=True)
            with pe.Fori(0, NPG // 2) as i:
                for b in range(2):
                    g = 2 * i + b
                    pe.wait_ge(oh_ready, g + 1)
                    pe.sem_inc(passed["pe"], 1)
                    for k in range(PG):
                        ins = nc.tensor.matmul(bank[3][:, 0:NT], oh_lo[:, b, k, :],
                                               oh_hi_s[:, bass.ds(g * PG + k, 1), :].rearrange("p a h -> p (a h)"),
                                               start=False, stop=False, skip_group_check=True)
                    ins.then_inc(oh_used, 1)
            pe.wait_ge(dve_pre, 3)

            def look(i, b):
                g = 2 * i + b
                pe.wait_ge(oh_ready, NPG + g + 1)
                pe.wait_ge(look_used, g + 1)
                pe.sem_inc(passed["pe"], 1)
                for k in range(PG):
                    ins = nc.tensor.transpose(bank[4 + b][:, k * P // 2:(k + 1) * P // 2].bitcast(BF16),
                                              oh_lo[:, b, k, :], identb[:, :])
                ins.then_inc(ohT_ps, 1)
                pe.wait_ge(ohT_sb, g + 1)
                pe.sem_inc(passed["pe"], 1)
                for k in range(PG):
                    for q in range(2):
                        ins = nc.tensor.matmul(bank[6 + b][:, k * NT:(k + 1) * NT], oh_loT[:, b, k, :],
                                               degp[:, q, :], start=q == 0, stop=q == 1)
                ins.then_inc(look_ps, 1)

            with pe.Fori(0, NPG // 2) as i:
                for b in range(2):
                    look(i, b)
            pe.wait_ge(dve_pre, 5)
            nc.tensor.matmul(bank[0][:, 0:4 * NT], zeros_b, zeros_b[:, 0:4 * NT], start=True, stop=False, skip_group_check=True)
            with pe.Fori(0, NPG // 2) as i:
                for b in range(2):
                    g = 2 * i + b
                    pe.wait_ge(oh_ready, 2 * NPG + 1 + g + 1)
                    pe.sem_inc(passed["pe"], 1)
                    for k in range(PG):
                        ins = nc.tensor.matmul(bank[0][:, 0:4 * NT], oh_lo[:, b, k, :],
                                               wparts[:, b, k, :, :].rearrange("p q h -> p (q h)"),
                                               start=False, stop=False, skip_group_check=True)
                    ins.then_inc(oh_used, 1)
            pe.wait_ge(dve_pre, 8)
            nc.tensor.matmul(bank[4][:, 0:1], h0[0:1, :], ones[0:1, 0:1], start=True, stop=True).then_inc(pe_pre, 1)
            pe.wait_ge(dve_pre, 9)
            nc.tensor.matmul(bank[5][:, 0:D], h0b, w1s, start=True, stop=True).then_inc(pe_pre, 1)
            pe.sem_inc(rows_free, 2)
            pe.sem_clear(passed["pe"])

            def new_tile(j, n):
                pe.wait_ge(h_sb, n + j + 1)
                if j:
                    pe.wait_ge(new_sb, n + j)
                pe.sem_inc(passed["pe"], 1)
                nc.tensor.transpose(bank[7][:, 0:P], xt[:, j, 0:D], identf[:, :]).then_inc(new_ps, 1)

            def ai_tile(j, n):
                pe.wait_ge(new_sb, n + j + 1)
                if j >= 2:
                    pe.wait_ge(row_done, n + j - 1)
                pe.sem_inc(passed["pe"], 1)
                o = bank[2 + j % 2]
                for h in range(H):
                    nc.tensor.matmul(o[:, h * P:(h + 1) * P], vb[:, h, :], hT[:, 2 + j % 2, :], start=True, stop=True)
                nc.tensor.matmul(o[:, 2 * P:2 * P + 4], hT[:, 2 + j % 2, :], v4n[:, :], start=True, stop=True)\
                    .then_inc(ai_ps, 1)

            def gcn_chunk(i, b, q, c):
                pe.wait_ge(gath[b], (i + 1) * 16 * K)
                for g in range(NG):
                    pe.wait_ge(oh_f, q * NG + g + 1)
                    pe.wait_ge(sums_free, q * NG + g + 1)
                    pe.sem_inc(passed["pe"], 1)
                    for k in range(GRP):
                        ins = nc.tensor.matmul(grp_sum((b + g) % 2, k)[:, 0:WIN], rows[:, b, g * GRP + k, 0:D],
                                               pw[:, (b + g) % 2, k, 0, :], start=True, stop=True)
                    ins.then_inc(sums, 1)
                pe.wait_ge(sums, q * NG + NG)
                pe.sem_inc(rows_free, 1)

            chunk_pairs(pe, 0, gcn_chunk)
            pe.wait_ge(chunk_done, CHUNKS)
            for j in range(NT):
                if j >= 2:
                    pe.wait_ge(y_sb, j - 1)
                nc.tensor.matmul(bank[4 + j % 2][:, 0:D], acc[:, 0, j * P:(j + 1) * P], w2s, start=True, stop=True)\
                    .then_inc(y_ps, 1)
            pe.wait_ge(vb_ready, 1)
            for s in range(NT + 1):
                if s < NT:
                    new_tile(s, 0)
                if s >= 1:
                    ai_tile(s - 1, 0)

            def gat(layer, final):
                def body(i, b, q, c):
                    cq = layer * CHUNKS + c
                    pe.wait_ge(al_ready, cq + 1)
                    pe.sem_inc(passed["pe"], 1)
                    nc.tensor.transpose(bank[4][0:HK, 0:P], alpha[:, b, :, :].rearrange("p h k -> p (h k)"),
                                        identf[:, :]).then_inc(al_ps, 1)
                    pe.wait_ge(scan1, cq + 1)
                    pe.sem_inc(passed["pe"], 1)
                    nc.tensor.matmul(bank[5][0:1, 0:HK], fwd[:, P - 1:P], identf[0:HK, 0:HK], start=True, stop=True)
                    nc.tensor.matmul(bank[5][0:1, 64:64 + HK], bwd[:, 0:1], identf[0:HK, 0:HK], start=True, stop=True)\
                        .then_inc(row_ps, 1)
                    pe.wait_ge(scan2, cq + 1)
                    pe.sem_inc(passed["pe"], 1)
                    for s in range(2):
                        ins = nc.tensor.matmul(bank[5][0:HK, 128 + s:129 + s], cin[0:1, s, :], ones[0:1, 0:1],
                                               start=True, stop=True)
                    ins.then_inc(col_ps, 1)
                    pe.wait_ge(expd, 2 * cq + 1)
                    pe.sem_inc(passed["pe"], 1)
                    nc.tensor.matmul(bank[7][:, 0:H], ones[0:1, :], phi[0:1, 1, :], start=True, stop=True)\
                        .then_inc(phi_ps, 1)
                    pe.wait_ge(expd, 2 * cq + 2)
                    pe.sem_inc(passed["pe"], 1)
                    nc.tensor.transpose(bank[6][:, 0:HK], bwd[:, :], identf[0:HK, 0:HK])
                    nc.tensor.transpose(bank[6][:, HK:2 * HK], fwd[:, :], identf[0:HK, 0:HK]).then_inc(t_ps, 1)
                    pe.wait_ge(gath[b], (layer * (CHUNKS // 2) + i + CHUNKS // 2 + 1) * 16 * K)
                    pe.wait_ge(est_ready, cq + 1)
                    pe.sem_inc(passed["pe"], 1)
                    for g in range(NG):
                        pe.wait_ge(p_ready, cq * NG + g + 1)
                        pe.wait_ge(oh_f, q * NG + g + 1)
                        pe.wait_ge(sums_free, q * NG + g + 1)
                        pe.sem_inc(passed["pe"], 1)
                        for k in range(GRP):
                            t = g * GRP + k
                            o = grp_sum((b + g) % 2, k)
                            w = pw[:, (b + g) % 2, k, :, :].rearrange("p r w -> p (r w)")
                            nc.tensor.matmul(o[:, 0:2 * WIN], rows[:, b, t, 0:D], w[:, 0:2 * WIN],
                                             start=True, stop=True)
                            ins = nc.tensor.matmul(o[0:EC, 2 * WIN:5 * WIN], edge_st[:, t, :], w,
                                                   start=True, stop=True)
                        ins.then_inc(sums, 1)
                    pe.wait_ge(sums, q * NG + NG)
                    pe.sem_inc(rows_free, 1)
                chunk_pairs(pe, q0(layer), body, peel=True)

                pe.wait_ge(chunk_done, q0(layer) + CHUNKS)
                pe.sem_inc(passed["pe"], 1)
                for j in range(NT):
                    jb = slice(j * P, (j + 1) * P)
                    for h in range(H):
                        nc.tensor.matmul(bank[7][:, NS0 + 4 * j + h:NS0 + 1 + 4 * j + h], acc[0:EC, 2 + h, jb],
                                         identf[0:EC, FA:FA + 1], start=True, stop=True)
                    ins = nc.tensor.matmul(bank[7][:, NS0 + 2 + 4 * j:NS0 + 4 + 4 * j], acc[0:EC, 4, jb],
                                           identf[0:EC, FA + 1:EC], start=True, stop=True)
                ins.then_inc(nsc_ps, 1)
                pe.wait_ge(xt_in, 16 * (layer + 2))
                pe.wait_ge(lay_w, 64 * (layer + 1))
                pe.sem_inc(passed["pe"], 1)
                n = n0(layer + 1)

                def old_tile(j):
                    if j:
                        pe.wait_ge(old_sb, n0(layer) + j)
                        pe.sem_inc(passed["pe"], 1)
                    nc.tensor.transpose(bank[6][:, 0:P], xt[:, j, 0:D], identf[:, :]).then_inc(old_ps, 1)

                old_tile(0)
                for s in range(NT + (0 if final else 2)):
                    jb, yb = slice(s * P, (s + 1) * P), bank[4 + s % 2]
                    if s < NT:
                        if s >= 2:
                            pe.wait_ge(y_sb, n + s - 1)
                            pe.sem_inc(passed["pe"], 1)
                        for h in range(H):
                            nc.tensor.matmul(yb[:, h * D:(h + 1) * D], acc[:, h, jb], Wl[:, h * D:(h + 1) * D],
                                             start=True, stop=False)
                            nc.tensor.matmul(yb[:, h * D:(h + 1) * D], acc[0:FA, 2 + h, jb],
                                             El[:, h * D:(h + 1) * D], start=False, stop=True)
                    if not final and 0 <= s - 2 < NT:
                        if s == 2:
                            pe.wait_ge(vb_ready, layer + 2)
                        ai_tile(s - 2, n)
                    if s < NT:
                        pe.wait_ge(old_sb, n0(layer) + s + 1)
                        pe.sem_inc(passed["pe"], 1)
                        nc.tensor.matmul(yb[:, 2 * D:4 * D], hT[:, s % 2, :], Wl[:, :], start=True, stop=True)\
                            .then_inc(y_ps, 1)
                    if not final and 0 <= s - 1 < NT:
                        new_tile(s - 1, n)
                    if s + 1 < NT:
                        old_tile(s + 1)

            rounds(pe, gat)

        @block.vector
        def _(v):
            steps = [0]

            def link(ins):
                steps[0] += 1
                ins.then_inc(step, 1)
                v.wait_ge(step, steps[0])

            def unlink():
                v.sem_clear(step)
                steps[0] = 0

            V = nc.vector
            V.memset(eps[:, :], LN_EPS)
            link(V.memset(zeros_b, 0.0))
            v.wait_ge(loaded, N_LOADS)
            v.wait_ge(made, 4)
            link(V.tensor_copy(row0_f[0:1, :], row0_i[0:1, :]))
            link(V.tensor_copy(row1_f[0:1, :], row1_i[0:1, :]))
            link(V.tensor_copy(identb[:, :], identf[:, :]))
            v.sem_inc(dve_pre, 1)
            for n in range(LAYERS * H):
                l, h = divmod(n, H)
                if n:
                    v.wait_ge(pe_pre, n + 1)
                link(V.tensor_scalar(attb, ones[:, :], attTs[:, l, 2 * h + 1:2 * h + 2], None, ALU.mult))
                v.sem_inc(att_spread, 1)
            link(V.tensor_copy(edge[:, :, :], attr_in))
            link(V.memset(edge_st[:, :, :], 1.0))
            for dup, t0, n in ((0, 0, TILES), (TILES, 0, 2 * K)):
                link(V.tensor_scalar(bases[0:1, dup:dup + n], row0_f[0:1, t0:t0 + n], float(LAST_BASE), None, ALU.min))
            link(V.tensor_tensor(r_e[0:1, :], row1_f[0:1, 0:TILES], row1_f[0:1, 1:TILES + 1], ALU.not_equal))
            link(V.tensor_scalar(row_start[0:1, :], r_e[0:1, :], -BIG, None, ALU.mult))
            link(V.tensor_tensor(r_e[0:1, :], row0_f[0:1, 0:TILES], row0_f[0:1, 1:TILES + 1], ALU.not_equal))
            link(V.tensor_scalar(row_end[0:1, :].rearrange("p (c k) -> p c k", k=K)[:, :, ::-1],
                                 r_e[0:1, :].rearrange("p (c k) -> p c k", k=K), -BIG, None, ALU.mult))
            v.wait_ge(loaded_rows, 16 * 6)
            for other, flags in ((rprev, start_add), (rnext, end_add)):
                link(V.tensor_tensor(flags[:, :, :] if flags is start_add else flags[:, :, ::-1],
                                     rcur[0:HK], other[0:HK], ALU.not_equal))
                link(V.tensor_scalar(flags[:, :, :], flags[:, :, :], -BIG, None, ALU.mult))
            v.wait_ge(pe_pre, 1 + LAYERS * H)
            link(V.tensor_copy(dst_f, dstc_i))
            link(V.tensor_copy(dstn_f, dstn_i))
            link(V.tensor_tensor(last_col[:, :], dst_f, dstn_f, ALU.not_equal))
            link(V.tensor_tensor(r_e, dst_f, bank[1][:, 0:TILES], ALU.subtract))
            link(V.tensor_copy(dstn_f[:, 0:P], iota_i))
            link(V.tensor_copy(iota_b, dstn_f[:, 0:P]))
            link(V.tensor_tensor(onehot[:, :, :], r_e.unsqueeze(2).broadcast_to((P, TILES, WIN)),
                                 dstn_f[:, 0:WIN].unsqueeze(1).broadcast_to((P, TILES, WIN)), ALU.is_equal))
            link(V.tensor_copy(V4[:, :, :].rearrange("p l q -> p (l q)"), bank[0][:, 0:LAYERS * 4]))
            link(V.tensor_copy(v17[:, :, :, :].rearrange("p l h k -> p (l h k)"),
                               bank[2][:, 0:LAYERS * H * (FA + 1)]))
            for key, lo, hi, oh in ((key_i, lo_s, hi_s, oh_hi_s), (dstc_i, lo_d, hi_d, oh_hi_d)):
                link(V.tensor_scalar(lo_i, key, P - 1, None, ALU.bitwise_and))
                link(V.tensor_scalar(hi_i, key, 7, None, ALU.arith_shift_right))
                link(V.tensor_copy(lo[:, 0:TILES], lo_i))
                link(V.tensor_copy(hi, hi_i))
                link(V.tensor_tensor(oh, hi.unsqueeze(2).broadcast_to((P, TILES, NT)),
                                     iota_b[:, 0:NT].unsqueeze(1).broadcast_to((P, TILES, NT)), ALU.is_equal))
            link(V.memset(lo_s[:, TILES:TILES + PG], 0.0))
            v.sem_inc(dve_pre, 1)
            v.sem_inc(look_used, 2)
            unlink()

            def lo_onehot(b, g, lo):
                link(V.tensor_tensor(oh_lo[:, b, :, :],
                                     lo[:, bass.ds(g * PG, PG)].unsqueeze(2).broadcast_to((P, PG, P)),
                                     iota_b.unsqueeze(1).broadcast_to((P, PG, P)), ALU.is_equal))

            PE_A = 1 + LAYERS * H
            v.sem_inc(oh_used, 2)
            with v.Fori(0, NPG // 2) as i:
                for b in range(2):
                    g = 2 * i + b
                    unlink()
                    v.wait_ge(oh_used, g + 1)
                    v.sem_inc(passed["dve"], 1)
                    lo_onehot(b, g, lo_s)
                    v.sem_inc(oh_ready, 1)
            v.wait_ge(oh_used, NPG + 2)
            unlink()
            link(V.tensor_copy(norm_src, bank[3][:, 0:NT]))
            link(V.tensor_copy(deg_i[:, 0, :], norm_src))
            link(V.tensor_scalar(deg_i[:, 1, :], deg_i[:, 0, :], 255, None, ALU.bitwise_and))
            link(V.tensor_tensor(deg_i[:, 2, :], deg_i[:, 0, :], deg_i[:, 1, :], ALU.subtract))
            link(V.tensor_copy(degp[:, 0, :], deg_i[:, 1, :]))
            link(V.tensor_copy(degp[:, 1, :], deg_i[:, 2, :]))
            link(V.tensor_scalar(norm_src, norm_src, 1.0, None, ALU.max))
            v.sem_inc(dve_pre, 1)
            unlink()
            lo_onehot(0, 0, lo_s)
            v.sem_inc(oh_ready, 1)
            with v.Fori(0, NPG // 2) as i:
                for b in range(2):
                    g = 2 * i + b
                    unlink()
                    lo_onehot(1 - b, g + 1, lo_s)
                    v.sem_inc(oh_ready, 1)
                    v.wait_ge(look_ps, g + 1)
                    v.sem_inc(passed["dve"], 1)
                    link(V.tensor_tensor(picked, bank[6 + b][:, 0:PG * NT].rearrange("p (t h) -> p t h", t=PG),
                                         oh_hi_s[:, bass.ds(g * PG, PG), :], ALU.mult))
                    link(V.tensor_reduce(deg_e[:, bass.ds(g * PG, PG)], picked, AX, ALU.add))
                    v.sem_inc(look_used, 1)
            unlink()
            link(V.tensor_scalar(n_e, deg_e, 1.0, None, ALU.max))
            v.sem_inc(dve_pre, 1)
            v.wait_ge(act_pre, 1)
            link(V.reciprocal(n_e, n_e))
            link(V.tensor_copy(parts4[:, :, 0], n_e))
            link(V.tensor_tensor(n_e, n_e, parts4[:, :, 0], ALU.subtract))
            link(V.tensor_copy(parts4[:, :, 1], n_e))
            link(V.tensor_tensor(n_e, n_e, parts4[:, :, 1], ALU.subtract))
            link(V.tensor_copy(parts4[:, :, 2], n_e))
            link(V.memset(parts4[:, :, 3], 1.0))
            v.sem_inc(dve_pre, 1)
            unlink()
            with v.Fori(0, NPG // 2) as i:
                for b in range(2):
                    g = 2 * i + b
                    unlink()
                    v.wait_ge(oh_used, NPG + g + 1)
                    v.sem_inc(passed["dve"], 1)
                    lo_onehot(b, g, lo_d)
                    link(V.tensor_tensor(
                        wparts[:, b, :, :, :],
                        oh_hi_d[:, bass.ds(g * PG, PG), :].unsqueeze(2).broadcast_to((P, PG, 4, NT)),
                        parts4[:, bass.ds(g * PG, PG), :].unsqueeze(3).broadcast_to((P, PG, 4, NT)), ALU.mult))
                    v.sem_inc(oh_ready, 1)
            v.wait_ge(oh_used, 2 * NPG + 2)
            unlink()
            link(V.tensor_copy(s_deg, bank[0][:, 0:4 * NT]))
            link(V.tensor_tensor(s_deg[:, NT:2 * NT], s_deg[:, NT:2 * NT], s_deg[:, 2 * NT:3 * NT], ALU.add))
            link(V.tensor_tensor(s_nd, s_deg[:, 0:NT], s_deg[:, NT:2 * NT], ALU.add))
            link(V.tensor_scalar(noedge[:, :], s_deg[:, 3 * NT:4 * NT], 0.0, -BIG, ALU.is_equal, ALU.mult))
            link(V.tensor_copy(norm_dst[:, :], s_deg[:, 3 * NT:4 * NT]))
            link(V.tensor_scalar(s_deg[:, 3 * NT:4 * NT], s_deg[:, 3 * NT:4 * NT], 1.0, None, ALU.max))
            link(V.bn_stats(stat[0:1, :], xrow[0:1, :]))
            link(V.bn_aggr(mv[0:1, 0:2], stat[0:1, :]))
            v.sem_inc(dve_pre, 1)
            v.wait_ge(act_pre, 4)
            link(V.reciprocal(norm_dst[:, :], s_deg[:, 3 * NT:4 * NT]))
            link(V.reciprocal(norm_src, norm_src))
            link(V.tensor_tensor(s_nd, s_nd, norm_dst[:, :], ALU.mult))
            v.sem_inc(dve_pre, 1)
            link(V.reciprocal(mv[0:1, 3:4], mv[0:1, 2:3]))
            link(V.tensor_scalar(h0[0:1, :], xrow[0:1, :], mv[0:1, 0:1], mv[0:1, 3:4], ALU.subtract, ALU.mult))
            link(V.tensor_scalar(h0[0:1, :], h0[0:1, :], 0.0, None, ALU.max))
            v.sem_inc(dve_pre, 1)
            v.wait_ge(pe_pre, PE_A + 1)
            link(V.tensor_copy(h0T, bank[4][:, 0:1]))
            link(V.tensor_scalar(h0b, ones[:, :], h0T, None, ALU.mult))
            v.sem_inc(dve_pre, 1)
            v.wait_ge(pe_pre, PE_A + 2)
            link(V.tensor_copy(gs, bank[5][:, 0:D]))
            link(V.memset(xt[:, :, D:ROW], 0.0))
            v.sem_inc(dve_pre, 1)
            for j in range(NT):
                if j >= 2:
                    v.wait_ge(act_pre, 5 + j - 2)
                link(V.scalar_tensor_tensor(out=y[:, j % 2, :], in0=gs, scalar=s_nd[:, j:j + 1], in1=b1s,
                                            op0=ALU.mult, op1=ALU.add))
                v.sem_inc(dve_pre, 1)
            v.wait_ge(act_pre, 4 + NT)
            for i in range(2):
                V.memset(bank[i][:, :], 0.0)
            V.memset(accf, 0.0)
            V.memset(brow[:, :, :], -BIG)
            for b in range(2):
                V.tensor_copy(idx_st[:, b, :], srci[:, b * K:(b + 1) * K])
                link(V.tensor_copy(base_st[:, b, :], bases[:, b * K:(b + 1) * K]))
            v.sem_inc(idx_ready, 2)
            v.sem_inc(sums_free, 2)
            unlink()

            def stage_idx(b, c):
                link(V.tensor_copy(idx_st[:, b, :], srci[:, bass.ds((c + 2) * K, K)]))
                v.sem_inc(idx_ready, 1)

            def stage_bases(b, c):
                link(V.tensor_copy(base_st[:, b, :], bases[:, bass.ds((c + 2) * K, K)]))

            def add_group(b, g, regs):
                for k in range(GRP):
                    t = g * GRP + k
                    base = nc.values_load(base_st[0:1, b, t:t + 1], engines=(mybir.EngineType.DVE,),
                                          min_val=0, max_val=LAST_BASE,
                                          skip_runtime_bounds_check_because="clamped on the chip")
                    win = acc[:, 0:regs, bass.ds(base, WIN)]
                    if t:
                        v.wait_ge(added, t)
                    V.tensor_tensor(win, win,
                                    grp_sum((b + g) % 2, k)[:, 0:regs * WIN].rearrange("p (r w) -> p r w", r=regs),
                                    ALU.add).then_inc(added, 1)

            def groups(b, q, regs, weigh):
                v.sem_clear(added)
                for g in range(2):
                    weigh(g)
                for g in range(NG):
                    v.wait_ge(sums, q * NG + g + 1)
                    v.sem_inc(passed["dve"], 1)
                    add_group(b, g, regs)
                    if g + 2 < NG:
                        weigh(g + 2)
                    v.wait_ge(added, (g + 1) * GRP)
                    v.sem_inc(sums_free, 1)

            def gcn_chunk(i, b, q, c):
                unlink()
                v.wait_ge(ee_free, q + 1)
                v.sem_inc(passed["dve"], 1)
                for l in range(LAYERS):
                    link(V.tensor_tensor(
                        prod, edge[:, bass.ds(c * K, K), :].unsqueeze(1).broadcast_to((P, H, K, FA)),
                        v17[:, l, :, 0:FA].unsqueeze(2).broadcast_to((P, H, K, FA)), ALU.mult))
                    link(V.tensor_reduce(ee_st[:, l, :, :].rearrange("p h k -> p (h k)"),
                                         prod.rearrange("p h k f -> p (h k) f"), AX, ALU.add))
                v.sem_inc(ee_ready, 1)
                v.wait_ge(gath[b], (i + 1) * 16 * K)
                v.sem_inc(passed["dve"], 1)
                stage_idx(b, c)
                groups(b, q, 1, lambda g: None)
                stage_bases(b, c)
                v.sem_inc(chunk_done, 1)

            chunk_pairs(v, 0, gcn_chunk)

            def publish(j, n):
                v.wait_ge(ai_sb, n + j + 1)
                v.sem_inc(passed["dve"], 1)
                link(V.tensor_tensor(node4[:, j, :], bank[2 + j % 2][:, 2 * P:2 * P + 4], v4c[:, :], ALU.add))
                V.tensor_copy(xt[:, j, D:ROW], node4[:, j, :].rearrange("p (h i) -> p i h", i=2)[:, 1, :])\
                    .then_inc(row_done, 1)

            def spread(layer):
                link(V.tensor_copy(v4n[:, :].unsqueeze(1), V4[:, bass.ds(layer, 1), :]))
                link(V.memset(v4c[:, :], 0.0))
                link(V.tensor_copy(v4c[:, :].rearrange("p (h i) -> p i h", i=2)[:, 1:2, :],
                                   v17[:, bass.ds(layer, 1), :, FA]))
                for h in range(H):
                    link(V.tensor_scalar(vb[:, h, :], ones[:, :], v4n[:, 2 * h:2 * h + 1], None, ALU.mult))
                v.sem_inc(vb_ready, 1)

            unlink()
            spread(0)
            v.wait_ge(xt_in, 16)
            for j in range(NT):
                v.wait_ge(y_ps, j + 1)
                V.scalar_tensor_tensor(out=y[:, j % 2, :], in0=bank[4 + j % 2][:, 0:D], scalar=norm_dst[:, j:j + 1],
                                       in1=b2s, op0=ALU.mult, op1=ALU.add).then_inc(y_sb, 1)
                v.wait_ge(y_sb, j + 1)
                link(V.scalar_tensor_tensor(out=xt[:, j, 0:D], in0=y[:, j % 2, :], scalar=0.0, in1=xt[:, j, 0:D],
                                            op0=ALU.max, op1=ALU.add))
                link(V.bn_stats(stat[:, :], xt[:, j, 0:D]))
                link(V.bn_aggr(sc[:, 0, j, :], stat[:, :]))
            v.sem_inc(x2_ready, 1)
            v.sem_inc(ln_stat, 1)
            v.wait_ge(ln_std, 1)
            link(V.reciprocal(sc[:, 2, :, 0], sc[:, 1, :, 0]))
            link(V.scalar_tensor_tensor(out=sc[:, 3, :, 0], in0=sc[:, 0, :, 0], scalar=-1.0, in1=sc[:, 2, :, 0],
                                        op0=ALU.mult, op1=ALU.mult))
            v.sem_inc(ln_coef, 1)
            for j in range(NT):
                publish(j, 0)
            v.sem_inc(win_used, 1)

            def gat(layer, final):
                unlink()
                link(V.memset(crow[:, :, :], -BIG))
                v.wait_ge(ee_in, 16 * (layer + 1))
                v.wait_ge(acc_zero, NT * (layer + 1))
                v.sem_inc(passed["dve"], 1)

                def ai_times(c, n):
                    v.wait_ge(win_ready, n + 1)
                    v.sem_inc(passed["dve"], 1)
                    link(V.tensor_tensor(ai_win[:, :, :, :], ai_win[:, :, :, :],
                                         onehot[:, bass.ds(c * K, K), :].unsqueeze(2).broadcast_to((P, K, H, WIN)),
                                         ALU.mult))

                def ai_sum(b, c):
                    link(V.tensor_reduce(alpha[:, b, :, :].rearrange("p h k -> p k h"), ai_win[:, :, :, :],
                                         AX, ALU.add))
                    v.sem_inc(win_used, 1)
                    link(V.tensor_tensor(alpha[:, b, :, :], alpha[:, b, :, :], ee[:, :, bass.ds(c * K, K)], ALU.add))

                ai_times(0, layer * CHUNKS)
                ai_sum(0, 0)

                def body(i, b, q, c):
                    cq = layer * CHUNKS + c
                    ahead = not (isinstance(c, int) and c == CHUNKS - 1)
                    unlink()
                    al_sb = alpha[:, b, :, :]
                    v.wait_ge(gath[b], (layer * (CHUNKS // 2) + i + CHUNKS // 2 + 1) * 16 * K)
                    v.sem_inc(passed["dve"], 1)
                    link(V.tensor_tensor(al_sb, al_sb, rows[:, b, :, D:ROW].rearrange("p k h -> p h k"), ALU.add))
                    V.scalar_tensor_tensor(out=al_sb, in0=al_sb, scalar=SLOPE, in1=al_sb,
                                           op0=ALU.mult, op1=ALU.max).then_inc(al_ready, 1)
                    stage_idx(b, c)
                    if ahead:
                        ai_times(c + 1, cq + 1)
                    v.wait_ge(al_ps, cq + 1)
                    v.sem_inc(passed["dve"], 1)
                    st = start_add[:, bass.ds(c, 1), :].rearrange("p a e -> p (a e)")
                    en = end_add[:, bass.ds(c, 1), :].rearrange("p a e -> p (a e)")
                    al = bank[4][0:HK, 0:P]
                    V.tensor_tensor_scan(fwd[:, :], st, al, -BIG, ALU.add, ALU.max)
                    V.tensor_tensor_scan(bwd[:, ::-1], en, al[:, ::-1], -BIG, ALU.add, ALU.max).then_inc(scan1, 1)
                    link(V.tensor_copy(crow[:, :, 0:1], crow[:, :, K:K + 1]))
                    if ahead:
                        ai_sum(1 - b, c + 1)
                    v.wait_ge(row_ps, cq + 1)
                    v.sem_inc(passed["dve"], 1)
                    for h in range(H):
                        V.tensor_tensor_scan(crow[:, h, 1:K + 1], row_start[:, bass.ds(c * K, K)],
                                             bank[5][0:1, h * K:(h + 1) * K], crow[:, h, 0:1], ALU.add, ALU.max)
                        ins = V.tensor_tensor_scan(brow[:, h, 0:K][:, ::-1], row_end[:, bass.ds(c * K, K)],
                                                   bank[5][0:1, 64 + h * K:64 + (h + 1) * K][:, ::-1], -BIG,
                                                   ALU.add, ALU.max)
                    link(ins)
                    V.tensor_copy(cin[:, 0, :].rearrange("p (h k) -> p h k", h=H), crow[:, :, 0:K])
                    V.tensor_copy(cin[:, 1, :].rearrange("p (h k) -> p h k", h=H), brow[:, :, 1:K + 1])\
                        .then_inc(scan2, 1)
                    link(V.tensor_tensor(phi[:, 0, :], crow[:, :, 0], brow[:, :, 0], ALU.max))
                    V.tensor_tensor(phi[:, 0, :], crow[:, :, 0], phi[:, 0, :], ALU.subtract).then_inc(diff, 1)
                    v.wait_ge(col_ps, cq + 1)
                    v.sem_inc(passed["dve"], 1)
                    link(V.tensor_copy(carry_col[:, :], bank[5][0:HK, 128:130]))
                    V.tensor_tensor_scan(fwd[:, :], st, al, carry_col[:, 0:1], ALU.add, ALU.max)
                    link(V.tensor_tensor_scan(bwd[:, ::-1], en, al[:, ::-1], carry_col[:, 1:2], ALU.add, ALU.max))
                    link(V.tensor_tensor(fwd[:, :], fwd[:, :], bwd[:, :], ALU.max))
                    V.tensor_tensor(bwd[:, :], al, fwd[:, :], ALU.subtract).then_inc(diff, 1)
                    v.wait_ge(phi_ps, cq + 1)
                    v.sem_inc(passed["dve"], 1)
                    first = nc.values_load(base_st[0:1, b, 0:1], engines=(mybir.EngineType.DVE,), min_val=0,
                                           max_val=LAST_BASE, skip_runtime_bounds_check_because="clamped on the chip")
                    for rg in (0, 2):
                        col = acc[:, rg:rg + 2, bass.ds(first, 1)]
                        link(V.tensor_tensor(col, col, bank[7][:, 0:H].unsqueeze(2), ALU.mult))
                    v.wait_ge(t_ps, cq + 1)
                    v.sem_inc(passed["dve"], 1)
                    link(V.tensor_copy(p2[:, :, :], bank[6][:, 0:HK].rearrange("p (h k) -> p k h", h=H)))
                    link(V.tensor_tensor(edge_st[:, :, FA + 1:EC], bank[6][:, HK:2 * HK].rearrange("p (h k) -> p k h", h=H),
                                         last_col[:, bass.ds(c * K, K)].unsqueeze(2).broadcast_to((P, K, H)), ALU.mult))

                    def weigh(g):
                        V.tensor_tensor(
                            pw[:, (b + g) % 2, :, 0:2, :],
                            onehot[:, bass.ds(c * K + g * GRP, GRP), :].unsqueeze(2).broadcast_to((P, GRP, H, WIN)),
                            p2[:, g * GRP:(g + 1) * GRP, :].unsqueeze(3).broadcast_to((P, GRP, H, WIN)), ALU.mult)\
                            .then_inc(p_ready, 1)

                    groups(b, q, REG, weigh)
                    stage_bases(b, c)
                    v.sem_inc(chunk_done, 1)

                chunk_pairs(v, q0(layer), body, peel=True)
                unlink()
                nh = (P, NT, H)
                n4 = node4[:, :, :].rearrange("p j (h i) -> p j i h", i=2)
                a_self, m_new, d_e, d_s = (sc[:, k, :, :] for k in range(4))
                link(V.tensor_tensor(a_self, n4[:, :, 0, :], n4[:, :, 1, :], ALU.add))
                link(V.scalar_tensor_tensor(out=a_self, in0=a_self, scalar=SLOPE, in1=a_self,
                                            op0=ALU.mult, op1=ALU.max))
                v.wait_ge(nsc_ps, layer + 1)
                v.sem_inc(passed["dve"], 1)
                ns = bank[7][:, NS0:NS0 + 4 * NT].rearrange("p (j q) -> p j q", q=4)
                link(V.tensor_tensor(d_e, ns[:, :, 2:4], noedge[:, :].unsqueeze(2).broadcast_to(nh), ALU.add))
                link(V.tensor_copy(c1[:, :, :], ns[:, :, 0:2]))
                link(V.tensor_tensor(m_new, d_e, a_self, ALU.max))
                link(V.tensor_tensor(d_e, d_e, m_new, ALU.subtract))
                link(V.tensor_tensor(d_s, a_self, m_new, ALU.subtract))
                v.sem_inc(nsc_m, 1)
                v.wait_ge(lay_w, 64 * (layer + 1))
                v.sem_inc(passed["dve"], 1)
                for h in range(H):
                    link(V.scalar_tensor_tensor(out=biasl[:, :], in0=ebl[:, h * D:(h + 1) * D], scalar=1.0 / H,
                                                in1=biasl[:, :], op0=ALU.mult, op1=ALU.add))
                if not final:
                    spread(layer + 1)
                v.wait_ge(nsc_e, layer + 1)
                v.sem_inc(passed["dve"], 1)
                link(V.tensor_tensor(c1[:, :, :], c1[:, :, :], d_e, ALU.mult))
                link(V.tensor_tensor(c1[:, :, :], c1[:, :, :], d_s, ALU.add))
                link(V.tensor_scalar(c1[:, :, :], c1[:, :, :], SM_EPS, float(H), ALU.add, ALU.mult))
                link(V.reciprocal(m_new, c1[:, :, :]))
                link(V.tensor_tensor(c1[:, :, :], d_e, m_new, ALU.mult))
                link(V.tensor_tensor(c2[:, :, :], d_s, m_new, ALU.mult))
                if final:
                    v.wait_ge(xmid_in, 16)
                n = n0(layer + 1)
                for s in range(NT + (0 if final else 2)):
                    if not final and s >= 2:
                        publish(s - 2, n)
                    if s < NT:
                        yb, yj = bank[4 + s % 2], y[:, s % 2, :]
                        v.wait_ge(y_ps, n + s + 1)
                        if not final and s >= 2:
                            v.wait_ge(h_sb, n + s - 1)
                        v.sem_inc(passed["dve"], 1)
                        add = biasl[:, :]
                        for m, (cf, h) in enumerate(((c1, 0), (c1, 1), (c2, 0), (c2, 1))):
                            ins = V.scalar_tensor_tensor(out=yj, in0=yb[:, m * D:(m + 1) * D],
                                                         scalar=cf[:, s, h:h + 1], in1=add, op0=ALU.mult, op1=ALU.add)
                            if m < 3 or final:
                                link(ins)
                            add = yj
                        if final:
                            v.sem_inc(y_sb, 1)
                            V.tensor_tensor(xt[:, s, 0:D], yj, rows[:, 1, s, 0:D], ALU.add).then_inc(row_done, 1)
                        else:
                            ins.then_inc(y_sb, 1)

            rounds(v, gat)


_INS = ['x', 'src_rows', 'src_key', 'dst_col', 'dst_next_col', 'dst_flat', 'dst_first',
        'dst_before', 'attr', 'W1', 'b1', 'W2', 'b2',
        'weights', 'weightsT', 'attT', 'edge_w', 'edge_woT', 'biases', 'edge_b']


def kernel(x, src, dst, edge_attr_16, L0_gnn_W1, L0_gnn_b1, L0_gnn_W2, L0_gnn_b2, L1_gnn_weights, L1_gnn_atts,
           L1_gnn_biases, L1_gnn_edge_ws, L1_gnn_edge_bs):
    import numpy as np
    import concourse.bacc as bacc
    from concourse.bass_utils import run_bass_kernel_spmd

    x, src, dst, ea = (np.asarray(a) for a in (x, src, dst, edge_attr_16))
    w, att, eb = (np.asarray(a) for a in (L1_gnn_weights, L1_gnn_atts, L1_gnn_edge_bs))
    ew, bi = np.asarray(L1_gnn_edge_ws), np.asarray(L1_gnn_biases)
    slots = TILES * P

    def padded(a, n, fill):
        return np.concatenate([a, np.full((n - a.shape[0],) + a.shape[1:], fill, a.dtype)])

    def columns(a):
        a = a.reshape((TILES, P) + a.shape[1:])
        return np.ascontiguousarray(np.swapaxes(a, 0, 1)).reshape(P, -1)

    src0 = columns(padded(src, slots, 0))
    d1 = padded(dst, slots + 1, PAD_DST)
    flat = np.concatenate([np.full(1, PAD_DST - 1, dst.dtype), padded(dst, slots + P, PAD_DST)]).reshape(1, -1)
    arrays = dict(
        x=padded(x, NP, 0),
        src_rows=np.concatenate([src0, src0[:, :2 * K]], axis=1),
        src_key=columns(padded(src, slots, 4095)),
        dst_col=columns(d1[:slots]), dst_next_col=columns(d1[1:slots + 1]), dst_flat=flat,
        dst_first=flat[:, 1::P], dst_before=flat[:, 0:(TILES + 1) * P:P],
        attr=columns(padded(ea, slots, 0)),
        W1=np.asarray(L0_gnn_W1), b1=np.asarray(L0_gnn_b1), W2=np.asarray(L0_gnn_W2), b2=np.asarray(L0_gnn_b2),
        weights=w.reshape(LAYERS * D, H * D),
        weightsT=w.reshape(LAYERS, D, H, D).transpose(3, 0, 2, 1).reshape(D, -1),
        attT=att.reshape(LAYERS, H, 2, D).transpose(3, 0, 1, 2).reshape(D, -1),
        edge_w=ew.transpose(0, 2, 1).reshape(LAYERS * FA, H * D),
        edge_woT=np.concatenate([ew.reshape(LAYERS, H, D, FA), eb.reshape(LAYERS, H, D, 1)], axis=3)
        .transpose(2, 0, 1, 3).reshape(D, -1),
        biases=bi, edge_b=eb,
    )
    nc = bacc.Bacc("TRN2", target_bir_lowering=False, num_devices=1)
    feeds, args = {}, []
    for name in _INS:
        a = np.ascontiguousarray(arrays[name])
        feeds[f"in_{name}"] = a
        args.append(nc.dram_tensor(f"in_{name}", a.shape, mybir.dt.from_np(a.dtype), kind="ExternalInput").ap())
    result = nc.dram_tensor("result", (N, D), F32, kind="ExternalOutput").ap()
    program(nc, *args, result)
    r = run_bass_kernel_spmd(nc, [feeds], core_ids=[0])
    return r.results[0]["result"]
```
